# Optimizing a Trainium2 kernel written in Bass

```python
import numpy as np
import jax
import jax.numpy as jnp

def _softmax(x, axis=-1):
    return jax.nn.softmax(x, axis=axis)

def _gelu(x):
    return jax.nn.gelu(x, approximate=True)

def _silu(x):
    return jax.nn.silu(x)

def _sigmoid(x):
    return jax.nn.sigmoid(x)

def _layernorm(x, axis=-1, eps=1e-05):
    m = jnp.mean(x, axis=axis, keepdims=True)
    v = jnp.var(x, axis=axis, keepdims=True)
    return (x - m) / jnp.sqrt(v + eps)

def _scatter_add(tgt, idx, src, axis=0):
    return tgt.at[idx].add(src)

def _segment_sum(src, seg, n):
    return jax.ops.segment_sum(src, seg, n)
kernel_name = 'mk_dlrm_tower_d1_rec_r8_55c258'

def setup_inputs(seed: int=0):
    np.random.seed(seed)
    _w = jnp.asarray

    def _rec_inputs():
        import jax
        import jax.numpy as jnp
        _tk = jax.random.key(seed)
        ids = jnp.stack([jax.random.randint(jax.random.fold_in(_tk, 200 + f), (2048,), 0, v, jnp.int32) for f, v in enumerate([12500, 1250, 1000, 12500, 1250, 1250, 1000, 125000, 1000, 1000, 12500, 1000, 1250, 1000, 12500, 1000, 1250, 1000, 12500, 1000, 1000, 12500, 12500, 12500, 1250, 1250])], axis=1)
        tbl_0 = 0.05 * jax.random.normal(jax.random.fold_in(_tk, 500 + 0), (12500, 128), jnp.float32)
        tbl_1 = 0.05 * jax.random.normal(jax.random.fold_in(_tk, 500 + 1), (1250, 128), jnp.float32)
        tbl_2 = 0.05 * jax.random.normal(jax.random.fold_in(_tk, 500 + 2), (1000, 128), jnp.float32)
        tbl_3 = 0.05 * jax.random.normal(jax.random.fold_in(_tk, 500 + 3), (12500, 128), jnp.float32)
        tbl_4 = 0.05 * jax.random.normal(jax.random.fold_in(_tk, 500 + 4), (1250, 128), jnp.float32)
        tbl_5 = 0.05 * jax.random.normal(jax.random.fold_in(_tk, 500 + 5), (1250, 128), jnp.float32)
        tbl_6 = 0.05 * jax.random.normal(jax.random.fold_in(_tk, 500 + 6), (1000, 128), jnp.float32)
        tbl_7 = 0.05 * jax.random.normal(jax.random.fold_in(_tk, 500 + 7), (125000, 128), jnp.float32)
        tbl_8 = 0.05 * jax.random.normal(jax.random.fold_in(_tk, 500 + 8), (1000, 128), jnp.float32)
        tbl_9 = 0.05 * jax.random.normal(jax.random.fold_in(_tk, 500 + 9), (1000, 128), jnp.float32)
        tbl_10 = 0.05 * jax.random.normal(jax.random.fold_in(_tk, 500 + 10), (12500, 128), jnp.float32)
        tbl_11 = 0.05 * jax.random.normal(jax.random.fold_in(_tk, 500 + 11), (1000, 128), jnp.float32)
        tbl_12 = 0.05 * jax.random.normal(jax.random.fold_in(_tk, 500 + 12), (1250, 128), jnp.float32)
        tbl_13 = 0.05 * jax.random.normal(jax.random.fold_in(_tk, 500 + 13), (1000, 128), jnp.float32)
        tbl_14 = 0.05 * jax.random.normal(jax.random.fold_in(_tk, 500 + 14), (12500, 128), jnp.float32)
        tbl_15 = 0.05 * jax.random.normal(jax.random.fold_in(_tk, 500 + 15), (1000, 128), jnp.float32)
        tbl_16 = 0.05 * jax.random.normal(jax.random.fold_in(_tk, 500 + 16), (1250, 128), jnp.float32)
        tbl_17 = 0.05 * jax.random.normal(jax.random.fold_in(_tk, 500 + 17), (1000, 128), jnp.float32)
        tbl_18 = 0.05 * jax.random.normal(jax.random.fold_in(_tk, 500 + 18), (12500, 128), jnp.float32)
        tbl_19 = 0.05 * jax.random.normal(jax.random.fold_in(_tk, 500 + 19), (1000, 128), jnp.float32)
        tbl_20 = 0.05 * jax.random.normal(jax.random.fold_in(_tk, 500 + 20), (1000, 128), jnp.float32)
        tbl_21 = 0.05 * jax.random.normal(jax.random.fold_in(_tk, 500 + 21), (12500, 128), jnp.float32)
        tbl_22 = 0.05 * jax.random.normal(jax.random.fold_in(_tk, 500 + 22), (12500, 128), jnp.float32)
        tbl_23 = 0.05 * jax.random.normal(jax.random.fold_in(_tk, 500 + 23), (12500, 128), jnp.float32)
        tbl_24 = 0.05 * jax.random.normal(jax.random.fold_in(_tk, 500 + 24), (1250, 128), jnp.float32)
        tbl_25 = 0.05 * jax.random.normal(jax.random.fold_in(_tk, 500 + 25), (1250, 128), jnp.float32)
        _rk = jax.random.fold_in(_tk, 7)
        r_dense_features = -0.000520686 + 1.00062 * jax.random.normal(jax.random.fold_in(_rk, 101), (2048, 128), jnp.float32)
        W_top1 = 0.0405887 * jax.random.normal(jax.random.fold_in(_tk, 801), (607, 512), jnp.float32)
        W_top2 = 0.0441942 * jax.random.normal(jax.random.fold_in(_tk, 802), (512, 256), jnp.float32)
        W_top3 = 0.0625 * jax.random.normal(jax.random.fold_in(_tk, 803), (256, 1), jnp.float32)
        b_top1 = jnp.zeros((512,), jnp.float32)
        b_top2 = jnp.zeros((256,), jnp.float32)
        return (r_dense_features, ids, tbl_0, tbl_1, tbl_2, tbl_3, tbl_4, tbl_5, tbl_6, tbl_7, tbl_8, tbl_9, tbl_10, tbl_11, tbl_12, tbl_13, tbl_14, tbl_15, tbl_16, tbl_17, tbl_18, tbl_19, tbl_20, tbl_21, tbl_22, tbl_23, tbl_24, tbl_25, W_top1, b_top1, W_top2, b_top2, W_top3)
    r_dense_features, ids, tbl_0, tbl_1, tbl_2, tbl_3, tbl_4, tbl_5, tbl_6, tbl_7, tbl_8, tbl_9, tbl_10, tbl_11, tbl_12, tbl_13, tbl_14, tbl_15, tbl_16, tbl_17, tbl_18, tbl_19, tbl_20, tbl_21, tbl_22, tbl_23, tbl_24, tbl_25, W_top1, b_top1, W_top2, b_top2, W_top3 = _rec_inputs()

    def _L0_rec_setup():
        import jax, jax.numpy as jnp
        import numpy as np
        NUM_SPARSE = 26
        EMBED_DIM = 128
        BATCH = 2048
        key = jax.random.key(seed)
        k1, k2 = jax.random.split(key)
        dense_features = jax.random.normal(k1, (BATCH, EMBED_DIM), dtype=jnp.float32)
        sparse_features = jax.random.normal(k2, (BATCH, NUM_SPARSE, EMBED_DIM), dtype=jnp.float32)
        return {'dense_features': dense_features, 'sparse_features': sparse_features}
    _L0_rec_all = _L0_rec_setup()
    _L0_rec_in = {k: v for k, v in _L0_rec_all.items() if k in ()}
    del _L0_rec_all
    return {'r_dense_features': r_dense_features, 'ids': ids, 'tbl_0': tbl_0, 'tbl_1': tbl_1, 'tbl_2': tbl_2, 'tbl_3': tbl_3, 'tbl_4': tbl_4, 'tbl_5': tbl_5, 'tbl_6': tbl_6, 'tbl_7': tbl_7, 'tbl_8': tbl_8, 'tbl_9': tbl_9, 'tbl_10': tbl_10, 'tbl_11': tbl_11, 'tbl_12': tbl_12, 'tbl_13': tbl_13, 'tbl_14': tbl_14, 'tbl_15': tbl_15, 'tbl_16': tbl_16, 'tbl_17': tbl_17, 'tbl_18': tbl_18, 'tbl_19': tbl_19, 'tbl_20': tbl_20, 'tbl_21': tbl_21, 'tbl_22': tbl_22, 'tbl_23': tbl_23, 'tbl_24': tbl_24, 'tbl_25': tbl_25, 'W_top1': W_top1, 'b_top1': b_top1, 'W_top2': W_top2, 'b_top2': b_top2, 'W_top3': W_top3}

def reference(r_dense_features, ids, tbl_0, tbl_1, tbl_2, tbl_3, tbl_4, tbl_5, tbl_6, tbl_7, tbl_8, tbl_9, tbl_10, tbl_11, tbl_12, tbl_13, tbl_14, tbl_15, tbl_16, tbl_17, tbl_18, tbl_19, tbl_20, tbl_21, tbl_22, tbl_23, tbl_24, tbl_25, W_top1, b_top1, W_top2, b_top2, W_top3):
    import jax
    import jax.numpy as jnp

    def _L0_rec_ref(dense_features, sparse_features):
        import jax, jax.numpy as jnp
        import numpy as np
        NUM_SPARSE = 26
        EMBED_DIM = 128
        BATCH = 2048
        F = NUM_SPARSE + 1
        combined = jnp.concatenate([dense_features[:, None, :], sparse_features], axis=1)
        interactions = jnp.einsum('bfd,bgd->bfg', combined, combined)
        iu, ju = jnp.triu_indices(F, k=1)
        interactions_flat = interactions[:, iu, ju]
        return jnp.concatenate([dense_features, interactions_flat], axis=1)
    e = jnp.stack([tbl_0[ids[:, 0]], tbl_1[ids[:, 1]], tbl_2[ids[:, 2]], tbl_3[ids[:, 3]], tbl_4[ids[:, 4]], tbl_5[ids[:, 5]], tbl_6[ids[:, 6]], tbl_7[ids[:, 7]], tbl_8[ids[:, 8]], tbl_9[ids[:, 9]], tbl_10[ids[:, 10]], tbl_11[ids[:, 11]], tbl_12[ids[:, 12]], tbl_13[ids[:, 13]], tbl_14[ids[:, 14]], tbl_15[ids[:, 15]], tbl_16[ids[:, 16]], tbl_17[ids[:, 17]], tbl_18[ids[:, 18]], tbl_19[ids[:, 19]], tbl_20[ids[:, 20]], tbl_21[ids[:, 21]], tbl_22[ids[:, 22]], tbl_23[ids[:, 23]], tbl_24[ids[:, 24]], tbl_25[ids[:, 25]]], axis=1)
    z = _L0_rec_ref(r_dense_features, e)
    z = z.reshape(z.shape[0], -1)
    h = jnp.concatenate([z, r_dense_features], axis=1)
    h = jnp.maximum(h @ W_top1 + b_top1, 0.0)
    h = jnp.maximum(h @ W_top2 + b_top2, 0.0)
    y = h @ W_top3
    return y

_drawn_inputs = setup_inputs


def setup_inputs(seed=0):
    import zlib

    import numpy as np

    out = dict(_drawn_inputs(seed))
    spreads = {'b_top1': (0.0, 0.1), 'b_top2': (0.0, 0.1)}
    factors = {}
    for name, (base, spread) in spreads.items():
        noise = np.random.default_rng([zlib.crc32(name.encode()), seed]).standard_normal(out[name].shape)
        drawn = base * np.exp(spread * noise) if base else spread * noise
        out[name] = jnp.asarray(drawn.astype(out[name].dtype))
    for name, factor in factors.items():
        out[name] = (out[name] * factor).astype(out[name].dtype)
    return out
```

```python
import concourse.bass as bass
from concourse import mybir
from contextlib import ExitStack

F32 = mybir.dt.float32
F32R = mybir.dt.float32r
I32 = mybir.dt.int32
ALU = mybir.AluOpType
ACT = mybir.ActivationFunctionType

P = 128
TABLES = 26
FEATS = TABLES + 1
SLOTS = 28
WIDE = 32
TILES = 16
BLOCKS = TILES // 2
QUAD = 4
QUADS = SLOTS // QUAD
GROUP = 4
BATCH = 4
BATCHES = P // (GROUP * BATCH)
COLS = SLOTS // GROUP
HALF = P // GROUP
H1, H2 = 512, 256
K1, K2 = H1 // P, H2 // P
N = 2 * P


def dlrm(nc, x, ids, tables, w_dense, w_pairs, b1, w2, b2, w3, y):
    x_v = x.rearrange("(p t) d -> p t d", t=TILES)
    ids_v = ids.rearrange("(p t) f -> p t f", t=TILES)

    ctx = ExitStack()
    with ctx:
        def sb(name, shape, dt=F32):
            return ctx.enter_context(nc.sbuf_tensor(name, shape, dt))

        def pb(name, shape):
            return ctx.enter_context(nc.psum_tensor(name, shape, F32))

        def sem(name):
            return ctx.enter_context(nc.semaphore(name))

        idx = [sb(f"idx{i}", [P, TABLES], I32) for i in range(2)]
        rows = [sb(f"rows{i}", [P, FEATS, P]) for i in range(2)]
        et_hi = [sb(f"et_hi{i}", [P, P, WIDE], F32R) for i in range(2)]
        et_lo = [sb(f"et_lo{i}", [P, P, WIDE], F32R) for i in range(2)]
        xt_hi = sb("xt_hi", [P, GROUP, 2, HALF], F32R)
        xt_lo = sb("xt_lo", [P, GROUP, 2, HALF], F32R)
        gram = sb("gram", [P, SLOTS, 2 * HALF])
        pairs = sb("pairs", [P, GROUP, COLS, 2 * HALF])
        pairs_hi = sb("pairs_hi", [P, GROUP, COLS, 2 * HALF], F32R)
        pairs_lo = sb("pairs_lo", [P, GROUP, COLS, 2 * HALF], F32R)
        h1 = sb("h1", [P, K1, N])
        h2 = sb("h2", [P, K2, 2, P])
        y_sb = sb("y_sb", [P, TILES])
        w1 = sb("w1", [P, COLS + 2, H1])
        w1_hi = sb("w1_hi", [P, COLS + 1, H1], F32R)
        w1_lo = sb("w1_lo", [P, COLS + 1, H1], F32R)
        w2_sb = sb("w2_sb", [P, K1, H2])
        w3_sb = sb("w3_sb", [P, K2])
        b1_sb = sb("b1_sb", [P, K1])
        b2_sb = sb("b2_sb", [P, K2])
        ident = sb("ident", [P, P])

        ps_t = [pb(f"ps_t{i}", [P, QUAD, P]) for i in range(2)]
        ps_g = [pb(f"ps_g{i}", [P, BATCH * GROUP * SLOTS + 64]) for i in range(2)]
        ps_1 = pb("ps_1", [P, K1, N])
        ps_2 = pb("ps_2", [P, K2, N])
        ps_y = pb("ps_y", [P, 512])

        weights_in = sem("weights_in")
        ident_ready = sem("ident_ready")
        zeros_ready = sem("zeros_ready")
        w1_steps = sem("w1_steps")
        idx_in = [sem(f"idx_in{i}") for i in range(2)]
        x_in = [sem(f"x_in{i}") for i in range(2)]
        gathered = [[sem(f"gathered{i}_{q}") for q in range(QUADS)] for i in range(2)]
        transposed = sem("transposed")
        hi_ready = sem("hi_ready")
        lo_ready = sem("lo_ready")
        gram_ready = sem("gram_ready")
        gram_dve = sem("gram_dve")
        gram_act = sem("gram_act")
        pairs_in = [sem(f"pairs_in{i}") for i in range(GROUP)]
        pairs_hi_ready = sem("pairs_hi_ready")
        pairs_lo_ready = sem("pairs_lo_ready")
        layer1 = sem("layer1")
        h1_ready = sem("h1_ready")
        layer2 = sem("layer2")
        h2_ready = sem("h2_ready")
        layer3 = sem("layer3")
        y_ready = sem("y_ready")
        y_out = sem("y_out")

        def quad(q):
            return range(QUAD * q, min(QUAD * q + QUAD, FEATS))

        def quad_slots(t, q):
            return t[:, :, QUAD * q:QUAD * q + len(quad(q))].rearrange("p b f -> p f b")

        def stationary(t, g):
            return t[:, GROUP * g:GROUP * (g + 1), :].rearrange("p b f -> p (b f)")

        def moving(t, g):
            return t[:, GROUP * g:GROUP * (g + 1), 0:SLOTS]

        def strip_out(par, m, i):
            s0 = HALF * par + BATCH * m
            return gram[32 * i:32 * i + 32, :, s0:s0 + BATCH].rearrange("p g s -> p s g")

        def strip_in(m, i):
            a = ps_g[m % 2][32 * i:32 * i + 32, 0:BATCH * GROUP * SLOTS]
            return a.rearrange("p (s c g) -> p s c g", s=BATCH, c=GROUP)[:, :, i, :]

        block = ctx.enter_context(nc.Block())

        @block.sync
        def _(sp):
            def load_tile(par, tile):
                sp.dma_start(idx[par][:, :], ids_v[:, bass.ds(tile, 1), :].rearrange("p t f -> p (t f)")).then_inc(idx_in[par], 16)
                sp.dma_start(rows[par][:, 0, :], x_v[:, bass.ds(tile, 1), :].rearrange("p t d -> p (t d)")).then_inc(x_in[par], 16)

            def move_pairs(n):
                for i in range(GROUP):
                    sp.wait_ge(gram_dve if i < 2 else gram_act, 2 * BATCHES * (n + 1))
                    for j in range(GROUP):
                        sp.dma_start(pairs[32 * j:32 * j + 32, i, :, :],
                                     gram[32 * i:32 * i + 32, COLS * j:COLS * (j + 1), :]).then_inc(pairs_in[i], 16)

            load_tile(0, 0)
            load_tile(1, 1)
            sp.dma_start(w1[:, 0:COLS, :], w_pairs).then_inc(weights_in, 16)
            sp.dma_start(w1[:, COLS:COLS + 2, :], w_dense).then_inc(weights_in, 16)
            sp.dma_start(w2_sb[:, :, :], w2.rearrange("(k p) n -> p k n", p=P)).then_inc(weights_in, 16)
            sp.dma_start(b1_sb[:, :], b1).then_inc(weights_in, 16)
            sp.dma_start(b2_sb[:, :], b2).then_inc(weights_in, 16)
            sp.dma_start(w3_sb[:, :], w3).then_inc(weights_in, 16)
            with sp.Fori(0, BLOCKS - 1) as n:
                for par in range(2):
                    sp.wait_ge(transposed, 2 * QUADS * n + QUADS * (par + 1))
                    load_tile(par, 2 * n + 2 + par)
                move_pairs(n)
            move_pairs(BLOCKS - 1)
            sp.wait_ge(y_ready, BLOCKS + 1)
            sp.dma_start(y.rearrange("(p t) o -> p (t o)", t=TILES), y_sb[:, :]).then_inc(y_out, 16)
            sp.wait_ge(y_out, 16)

        @block.gpsimd
        def _(pool):
            pool.memset(ident[:, :], 0.0).then_inc(ident_ready, 1)
            pool.wait_ge(ident_ready, 1)
            pool.affine_select(out=ident[:, :], in_=ident[:, :], compare_op=ALU.not_equal, fill=1.0,
                               base=0, pattern=[[-1, P]], channel_multiplier=1).then_inc(ident_ready, 1)

            def gather_tile(par, uses, freed):
                pool.wait_ge(idx_in[par], 16 * uses)
                pool.nop(nofuse=True)
                for q in range(QUADS):
                    if freed is not None:
                        pool.wait_ge(transposed, freed + q + 1)
                        pool.nop(nofuse=True)
                    for f in quad(q):
                        if f:
                            pool.indirect_dma_start(
                                rows[par][:, f, :], None, tables[f - 1],
                                bass.IndirectOffsetOnAxis(idx[par][:, f - 1:f], 0)).then_inc(gathered[par][q], 16)

            for par in range(2):
                gather_tile(par, 1, None)
            with pool.Fori(0, BLOCKS - 1) as m:
                for par in range(2):
                    gather_tile(par, m + 2, 2 * QUADS * m + QUADS * par)

        @block.tensor
        def _(pe):
            pe.wait_ge(ident_ready, 2)
            pe.wait_ge(zeros_ready, 4)
            pe.wait_ge(w1_steps, 3)
            pe.wait_ge(weights_in, 6 * 16)
            with pe.Fori(0, BLOCKS) as n:
                for par in range(2):
                    for q in range(QUADS):
                        done = QUADS * par + q
                        if q == 0:
                            pe.wait_ge(x_in[par], 16 * (n + 1))
                        pe.wait_ge(gathered[par][q], 16 * (len(quad(q)) - (q == 0)) * (n + 1))
                        if done >= 2:
                            pe.wait_ge(lo_ready, 2 * QUADS * n + done - 1)
                        for f in quad(q):
                            last = nc.tensor.transpose(ps_t[done % 2][:, f % QUAD, :], rows[par][:, f, :], ident[:, :])
                        last.then_inc(transposed, 1)
                    pe.wait_ge(lo_ready, 2 * QUADS * n + QUADS * (par + 1))
                    for m in range(BATCHES):
                        done = BATCHES * par + m
                        if done >= 2:
                            pe.wait_ge(gram_dve, 2 * BATCHES * n + done - 1)
                            pe.wait_ge(gram_act, 2 * BATCHES * n + done - 1)
                        for s in range(BATCH):
                            g = BATCH * m + s
                            out = ps_g[done % 2][:, GROUP * SLOTS * s:GROUP * SLOTS * (s + 1)]
                            nc.tensor.matmul(out, stationary(et_hi[par], g), moving(et_hi[par], g), start=True, stop=False)
                            nc.tensor.matmul(out, stationary(et_hi[par], g), moving(et_lo[par], g), start=False, stop=False)
                            last = nc.tensor.matmul(out, stationary(et_lo[par], g), moving(et_hi[par], g), start=False, stop=True)
                        last.then_inc(gram_ready, 1)
                pe.wait_ge(pairs_lo_ready, GROUP * (n + 1))
                for h in range(K1):
                    hc = slice(P * h, P * h + P)
                    for k in range(COLS + 1):
                        if k < COLS:
                            hi, lo = pairs_hi[:, :, k, :], pairs_lo[:, :, k, :]
                        else:
                            hi = xt_hi[:, :, :, :].rearrange("p i t s -> p (i t s)")
                            lo = xt_lo[:, :, :, :].rearrange("p i t s -> p (i t s)")
                        nc.tensor.matmul(ps_1[:, h, :], w1_hi[:, k, hc], hi, start=(k == 0), stop=False)
                        nc.tensor.matmul(ps_1[:, h, :], w1_hi[:, k, hc], lo, start=False, stop=False)
                        last = nc.tensor.matmul(ps_1[:, h, :], w1_lo[:, k, hc], hi, start=False, stop=(k == COLS))
                    if h % 2:
                        last.then_inc(layer1, 1)
                pe.wait_ge(h1_ready, K1 * (n + 1))
                for h in range(K2):
                    for k in range(K1):
                        last = nc.tensor.matmul(ps_2[:, h, :], w2_sb[:, k, P * h:P * h + P], h1[:, k, :],
                                                start=(k == 0), stop=(k == K1 - 1))
                last.then_inc(layer2, 1)
                pe.wait_ge(h2_ready, K2 * (n + 1))
                pe.wait_ge(y_ready, n + 1)
                for t in range(2):
                    for k in range(K2):
                        last = nc.tensor.matmul(ps_y[:, t:t + 1], h2[:, k, t, :], w3_sb[:, k:k + 1], start=(k == 0), stop=(k == K2 - 1))
                last.then_inc(layer3, 1)

        @block.scalar
        def _(act):
            act.wait_ge(w1_steps, 1)
            nc.scalar.copy(w1_hi[:, :, :], w1[:, 0:COLS + 1, :]).then_inc(w1_steps, 1)
            with act.Fori(0, BLOCKS) as n:
                for par in range(2):
                    for q in range(QUADS):
                        act.wait_ge(transposed, 2 * QUADS * n + QUADS * par + q + 1)
                        bank = ps_t[(QUADS * par + q) % 2]
                        if q == 0:
                            nc.scalar.copy(xt_hi[:, :, par, :], bank[:, 0, :].rearrange("p (s i) -> p i s", i=GROUP))
                        nc.scalar.copy(quad_slots(et_hi[par], q), bank[:, 0:len(quad(q)), :]).then_inc(hi_ready, 1)
                    for m in range(BATCHES):
                        act.wait_ge(gram_ready, 2 * BATCHES * n + BATCHES * par + m + 1)
                        nc.scalar.copy(strip_out(par, m, 2), strip_in(m, 2))
                        nc.scalar.copy(strip_out(par, m, 3), strip_in(m, 3)).then_inc(gram_act, 1)
                for i in range(GROUP):
                    act.wait_ge(pairs_in[i], 16 * GROUP * (n + 1))
                    nc.scalar.copy(pairs_hi[:, i, :, :], pairs[:, i, :, :]).then_inc(pairs_hi_ready, 1)
                for h in range(K1):
                    if h % 2 == 0:
                        act.wait_ge(layer1, K1 // 2 * n + h // 2 + 1)
                    nc.scalar.activation(h1[:, h, :], ps_1[:, h, :], ACT.Relu, bias=b1_sb[:, h:h + 1]).then_inc(h1_ready, 1)

        @block.vector
        def _(dve):
            for t in (et_hi, et_lo):
                for par in range(2):
                    nc.vector.memset(t[par][:, :, :].bitcast(F32), 0.0).then_inc(zeros_ready, 1)
            nc.vector.memset(y_sb[:, :], 0.0).then_inc(y_ready, 1)
            dve.wait_ge(weights_in, 6 * 16)
            nc.vector.tensor_tensor(w1[:, COLS, :], w1[:, COLS, :], w1[:, COLS + 1, :], ALU.add).then_inc(w1_steps, 1)
            dve.wait_ge(w1_steps, 2)
            nc.vector.tensor_tensor(w1_lo[:, :, :], w1[:, 0:COLS + 1, :], w1_hi[:, :, :].bitcast(F32), ALU.subtract).then_inc(w1_steps, 1)
            with dve.Fori(0, BLOCKS) as n:
                for par in range(2):
                    for q in range(QUADS):
                        dve.wait_ge(hi_ready, 2 * QUADS * n + QUADS * par + q + 1)
                        bank = ps_t[(QUADS * par + q) % 2]
                        if q == 0:
                            nc.vector.tensor_tensor(xt_lo[:, :, par, :], bank[:, 0, :].rearrange("p (s i) -> p i s", i=GROUP),
                                                    xt_hi[:, :, par, :].bitcast(F32), ALU.subtract)
                        nc.vector.tensor_tensor(quad_slots(et_lo[par], q), bank[:, 0:len(quad(q)), :],
                                                quad_slots(et_hi[par], q).bitcast(F32), ALU.subtract).then_inc(lo_ready, 1)
                    for m in range(BATCHES):
                        dve.wait_ge(gram_ready, 2 * BATCHES * n + BATCHES * par + m + 1)
                        nc.vector.tensor_copy(strip_out(par, m, 0), strip_in(m, 0))
                        nc.vector.tensor_copy(strip_out(par, m, 1), strip_in(m, 1)).then_inc(gram_dve, 1)
                for i in range(GROUP):
                    dve.wait_ge(pairs_hi_ready, GROUP * n + i + 1)
                    nc.vector.tensor_tensor(pairs_lo[:, i, :, :], pairs[:, i, :, :], pairs_hi[:, i, :, :].bitcast(F32),
                                            ALU.subtract).then_inc(pairs_lo_ready, 1)
                dve.wait_ge(layer2, n + 1)
                for h in range(K2):
                    nc.vector.tensor_scalar(h2[:, h, :, :].rearrange("p t (s i) -> p i t s", i=GROUP), ps_2[:, h, :].rearrange("p (i t s) -> p i t s", i=GROUP, t=2), b2_sb[:, h:h + 1], 0.0, ALU.add, ALU.max).then_inc(h2_ready, 1)
                dve.wait_ge(layer3, n + 1)
                nc.vector.tensor_copy(y_sb[:, bass.ds(2 * n, 2)], ps_y[:, 0:2]).then_inc(y_ready, 1)


def kernel(**inputs):
    import numpy as np
    import concourse.bacc as bacc
    from concourse.bass_utils import run_bass_kernel_spmd

    nc = bacc.Bacc("TRN2", target_bir_lowering=False, num_devices=1)
    w_top1 = np.asarray(inputs["W_top1"])
    f, g = np.triu_indices(FEATS, k=1)
    w_pairs = np.zeros((P, COLS, H1), w_top1.dtype)
    w_pairs[32 * (g // COLS) + f, g % COLS] = w_top1[P:P + len(f)]
    arrays = {
        "x": inputs["r_dense_features"], "ids": inputs["ids"], "w_pairs": w_pairs,
        "w_dense": np.stack([w_top1[0:P], w_top1[P + len(f):]], axis=1),
        "b1": np.asarray(inputs["b_top1"]).reshape(K1, P).T, "w2": inputs["W_top2"],
        "b2": np.asarray(inputs["b_top2"]).reshape(K2, P).T,
        "w3": np.asarray(inputs["W_top3"]).reshape(K2, P).T,
    }
    arrays.update({f"tbl_{i}": inputs[f"tbl_{i}"] for i in range(TABLES)})
    arrays = {k: np.ascontiguousarray(v) for k, v in arrays.items()}
    ap = {k: nc.dram_tensor(k, v.shape, mybir.dt.from_np(v.dtype), kind="ExternalInput").ap() for k, v in arrays.items()}
    y = nc.dram_tensor("y", (TILES * P, 1), F32, kind="ExternalOutput").ap()
    dlrm(nc, ap["x"], ap["ids"], [ap[f"tbl_{i}"] for i in range(TABLES)], ap["w_dense"], ap["w_pairs"],
         ap["b1"], ap["w2"], ap["b2"], ap["w3"], y)
    return run_bass_kernel_spmd(nc, [arrays], core_ids=[0]).results[0]["y"]
```

```python
import concourse.bass as bass
from concourse import mybir
from contextlib import ExitStack

F32 = mybir.dt.float32
F32R = mybir.dt.float32r
I32 = mybir.dt.int32
ALU = mybir.AluOpType
ACT = mybir.ActivationFunctionType

P = 128
TABLES = 26
FEATS = TABLES + 1
SELECTED = [2, 6, 8, 9, 11, 13]
GATHERED = [t for t in range(TABLES) if t not in SELECTED]
TILES = 16
BLOCKS = TILES // 2
N = 2 * P

SLOTS = 28
WIDE = 32
ROWS = 1 + len(GATHERED)
QUAD = 4
QUADS = -(-ROWS // QUAD)

SEL = len(SELECTED)
SEL_ROWS = 1000
CHUNK = 125
CHUNKS = SEL_ROWS // CHUNK
PAIRS = SEL // 2
ONE_HOTS = SEL * CHUNKS
RING = 16

GROUP = 4
BATCH = 4
BATCHES = P // (GROUP * BATCH)
COLS = SLOTS // GROUP
HALF = P // GROUP
H1, H2 = 512, 256
K1, K2 = H1 // P, H2 // P
KZ = COLS + 1


def dlrm(nc, x, ids, sel_ids, gathered_tables, selected_tables, w_dense, w_pairs, b1, w2, b2, w3, y):
    x_v = x.rearrange("(p t) d -> p t d", t=TILES)
    ids_v = ids.rearrange("(p t) f -> p t f", t=TILES)

    ctx = ExitStack()
    with ctx:
        def sb(name, shape, dt=F32):
            return ctx.enter_context(nc.sbuf_tensor(name, shape, dt))

        def pb(name, shape):
            return ctx.enter_context(nc.psum_tensor(name, shape, F32))

        def sem(name):
            return ctx.enter_context(nc.semaphore(name))

        idx = [sb(f"idx{i}", [P, TABLES], I32) for i in range(2)]
        rows = [sb(f"rows{i}", [P, ROWS, P]) for i in range(2)]
        et = sb("et", [P, 2, N, WIDE], F32R)
        table_hi = sb("table_hi", [CHUNK, SEL, CHUNKS, P], F32R)
        table_lo = sb("table_lo", [CHUNK, SEL, CHUNKS, P], F32R)
        sel_idx = sb("sel_idx", [CHUNK, SEL, N])
        first_row = sb("first_row", [CHUNK, 1])
        first_row_int = sb("first_row_int", [CHUNK, 1], I32)
        one_hot = sb("one_hot", [CHUNK, RING, N], F32R)
        w1 = sb("w1", [P, KZ + 1, H1])
        w2_sb = sb("w2_sb", [P, K1, H2])
        w3_sb = sb("w3_sb", [P, K2])
        b1_sb = sb("b1_sb", [P, K1])
        b2_sb = sb("b2_sb", [P, K2])
        y_sb = sb("y_sb", [P, TILES])
        ident = sb("ident", [P, P])
        work = sb("work", [P, SEL * CHUNKS * P])
        ends = [0]
        for size in (SLOTS * 2 * HALF, GROUP * KZ * 2 * HALF, K1 * N, K2 * N):
            ends.append(ends[-1] + size)
        assert ends[-1] <= SEL * CHUNKS * P
        gram = work[:, ends[0]:ends[1]].rearrange("p (g s) -> p g s", g=SLOTS)
        pairs = work[:, ends[1]:ends[2]].rearrange("p (i c s) -> p i c s", i=GROUP, c=KZ)
        h1 = work[:, ends[2]:ends[3]].rearrange("p (k n) -> p k n", k=K1)
        h2 = work[:, ends[3]:ends[4]].rearrange("p (k t b) -> p k t b", k=K2, t=2)

        ps_t = [pb(f"ps_t{i}", [P, QUAD, P]) for i in range(2)]
        ps_g = [pb(f"ps_g{i}", [P, BATCH, N]) for i in range(2)]
        ps_m = pb("ps_m", [P, K1, N])
        ps_2 = ps_m[:, 0:K2, :]
        ps_y = ps_m[:, K2, 0:2]

        weights_in = sem("weights_in")
        w1_ready = sem("w1_ready")
        ident_ready = sem("ident_ready")
        zeros_ready = sem("zeros_ready")
        first_row_ready = sem("first_row_ready")
        tables_in = [sem(f"tables_in{i}") for i in range(SEL)]
        tables_hi_ready = sem("tables_hi_ready")
        tables_ready = sem("tables_ready")
        idx_in = [sem(f"idx_in{i}") for i in range(2)]
        x_in = [sem(f"x_in{i}") for i in range(2)]
        gathered = [[sem(f"gathered{i}_{q}") for q in range(QUADS)] for i in range(2)]
        sel_idx_in = sem("sel_idx_in")
        sel_idx_ready = sem("sel_idx_ready")
        one_hot_ready = sem("one_hot_ready")
        one_hot_used = sem("one_hot_used")
        sel_hi = sem("sel_hi")
        sel_lo = sem("sel_lo")
        transposed = sem("transposed")
        et_hi = sem("et_hi")
        et_lo = sem("et_lo")
        gram_ready = sem("gram_ready")
        gram_half = sem("gram_half")
        gram_out = sem("gram_out")
        dense_ready = sem("dense_ready")
        pairs_in = [sem(f"pairs_in{i}") for i in range(GROUP)]
        layer1 = sem("layer1")
        h1_ready = sem("h1_ready")
        layer2 = sem("layer2")
        h2_ready = sem("h2_ready")
        layer3 = sem("layer3")
        y_ready = sem("y_ready")
        y_out = sem("y_out")

        def quad_bank(q):
            if q < 2:
                return ps_t[1 - q][:, :, :]
            return ps_g[q // 2 - 1][:, :, :].rearrange("p s c -> p (s c)")[:, 512 * (q % 2):512 * (q % 2 + 1)].rearrange(
                "p (q b) -> p q b", q=QUAD)

        def quad(q):
            return range(QUAD * q, min(QUAD * q + QUAD, ROWS))

        def quad_slots(part, par, q):
            return et[:, part, P * par:P * (par + 1), QUAD * q:QUAD * q + len(quad(q))].rearrange("p b f -> p f b")

        def sel_slots(part, k):
            return et[:, part, :, ROWS + 2 * k:ROWS + 2 * k + 2].rearrange("p b f -> p f b")

        def sel_bank(k):
            return ps_t[k % 2][:, :, :].rearrange("p q b -> p (q b)").rearrange("p (f b) -> p f b", f=2)

        def raw_table(i):
            return work[0:CHUNK, CHUNKS * P * i:CHUNKS * P * (i + 1)].rearrange("p (c d) -> p c d", c=CHUNKS)

        def gram_strip(par, m, i):
            s0 = HALF * par + BATCH * m
            return gram[32 * i:32 * i + 32, :, s0:s0 + BATCH].rearrange("p g s -> p s g")

        def diagonal(part, m, i):
            c = SLOTS * (GROUP * part + i)
            return ps_g[m % 2][32 * i:32 * i + 32, :, c:c + SLOTS]

        block = ctx.enter_context(nc.Block())

        @block.sync
        def _(sp):
            def load_tile(par, tile):
                sp.dma_start(idx[par][:, :], ids_v[:, bass.ds(tile, 1), :].rearrange("p t f -> p (t f)")).then_inc(idx_in[par], 16)
                sp.dma_start(rows[par][:, 0, :], x_v[:, bass.ds(tile, 1), :].rearrange("p t d -> p (t d)")).then_inc(x_in[par], 16)

            def load_sel_idx(n):
                src = sel_ids[bass.ds(n, 1), :, :].rearrange("n f b -> n (f b)").broadcast_to([CHUNK, SEL * N])
                sp.dma_start(sel_idx[:, :, :].bitcast(I32), src.rearrange("p (f b) -> p f b", f=SEL)).then_inc(sel_idx_in, 16)

            def move_pairs(n):
                sp.wait_ge(gram_out, 2 * BATCHES * (n + 1))
                for i in range(GROUP):
                    for j in range(GROUP):
                        sp.dma_start(pairs[32 * j:32 * j + 32, i, 0:COLS, :],
                                     gram[32 * i:32 * i + 32, COLS * j:COLS * (j + 1), :]).then_inc(pairs_in[i], 16)

            load_sel_idx(0)
            load_tile(0, 0)
            for i in range(SEL):
                sp.dma_start(raw_table(i), selected_tables[i].rearrange("(p c) d -> p c d", p=CHUNK)).then_inc(tables_in[i], 16)
            load_tile(1, 1)
            sp.dma_start(w1[:, 0:COLS, :], w_pairs).then_inc(weights_in, 16)
            sp.dma_start(w1[:, COLS:KZ + 1, :], w_dense).then_inc(weights_in, 16)
            sp.dma_start(w2_sb[:, :, :], w2.rearrange("(k p) n -> p k n", p=P)).then_inc(weights_in, 16)
            sp.dma_start(b1_sb[:, :], b1).then_inc(weights_in, 16)
            sp.dma_start(b2_sb[:, :], b2).then_inc(weights_in, 16)
            sp.dma_start(w3_sb[:, :], w3).then_inc(weights_in, 16)
            with sp.Fori(0, BLOCKS - 1) as n:
                sp.wait_ge(one_hot_ready, ONE_HOTS * (n + 1))
                load_sel_idx(n + 1)
                for par in range(2):
                    sp.wait_ge(transposed, QUADS * (2 * n + par + 1))
                    load_tile(par, 2 * n + 2 + par)
                move_pairs(n)
            move_pairs(BLOCKS - 1)
            sp.wait_ge(y_ready, BLOCKS + 1)
            sp.dma_start(y.rearrange("(p t) o -> p (t o)", t=TILES), y_sb[:, :]).then_inc(y_out, 16)
            sp.wait_ge(y_out, 16)

        @block.gpsimd
        def _(pool):
            pool.memset(ident[:, :], 0.0).then_inc(ident_ready, 1)
            pool.wait_ge(ident_ready, 1)
            pool.affine_select(out=ident[:, :], in_=ident[:, :], compare_op=ALU.not_equal, fill=1.0,
                               base=0, pattern=[[-1, P]], channel_multiplier=1).then_inc(ident_ready, 1)
            pool.iota(first_row_int[:, :], pattern=[[1, 1]], base=0, channel_multiplier=-CHUNKS).then_inc(first_row_ready, 1)

            def gather_tile(par, uses, freed):
                pool.wait_ge(idx_in[par], 16 * uses)
                pool.nop(nofuse=True)
                for q in range(QUADS):
                    if freed is not None:
                        pool.wait_ge(transposed, freed + q + 1)
                        pool.nop(nofuse=True)
                    for f in quad(q):
                        if f:
                            table = GATHERED[f - 1]
                            pool.indirect_dma_start(
                                rows[par][:, f, :], None, gathered_tables[f - 1],
                                bass.IndirectOffsetOnAxis(idx[par][:, table:table + 1], 0)).then_inc(gathered[par][q], 16)

            for par in range(2):
                gather_tile(par, 1, None)
            with pool.Fori(0, BLOCKS - 1) as m:
                for par in range(2):
                    gather_tile(par, m + 2, QUADS * (2 * m + par))

        @block.tensor
        def _(pe):
            def select(n):
                for c in range(ONE_HOTS):
                    k, f = c // (2 * CHUNKS), c // CHUNKS
                    if k >= 2 and c % (2 * CHUNKS) == 0:
                        pe.wait_ge(sel_lo, PAIRS * n + k - 1)
                    pe.wait_ge(one_hot_ready, ONE_HOTS * n + c + 1)
                    out = sel_bank(k)[:, f % 2, :]
                    nc.tensor.matmul(out, table_hi[:, f, c % CHUNKS, :], one_hot[:, c % RING, :],
                                     start=(c % CHUNKS == 0), stop=False)
                    nc.tensor.matmul(out, table_lo[:, f, c % CHUNKS, :], one_hot[:, c % RING, :],
                                     start=False, stop=(c % CHUNKS == CHUNKS - 1)).then_inc(one_hot_used, 1)

            def transpose_quad(n, par, q, later):
                if q == 0:
                    pe.wait_ge(x_in[par], 16 * (n + 1))
                pe.wait_ge(gathered[par][q], 16 * (len(quad(q)) - (q == 0)) * (n + 1))
                if par == 0 and q < 2:
                    pe.wait_ge(sel_lo, PAIRS * n + PAIRS - 1 + q)
                if (par or later) and q in (2, 4):
                    pe.wait_ge(gram_out, BATCHES * (2 * n + par) - 2 + q // 2)
                for f in quad(q):
                    last = nc.tensor.transpose(quad_bank(q)[:, f % QUAD, :], rows[par][:, f, :], ident[:, :])
                last.then_inc(transposed, 1)

            def gram_batch(n, par, m):
                if m == 0:
                    pe.wait_ge(et_lo, QUADS * (2 * n + par + 1))
                if m >= 2:
                    pe.wait_ge(gram_out, BATCHES * (2 * n + par) + m - 1)
                for s in range(BATCH):
                    b = P * par + GROUP * (BATCH * m + s)
                    last = nc.tensor.matmul(
                        ps_g[m % 2][:, s, 0:2 * GROUP * SLOTS].rearrange("p (a b f) -> p a b f", a=2, b=GROUP),
                        et[:, 0, b:b + GROUP, :].rearrange("p b f -> p (b f)"),
                        et[:, :, b:b + GROUP, 0:SLOTS], start=True, stop=True)
                last.then_inc(gram_ready, 1)

            def layer_1(n, start, end):
                for i in range(start, end):
                    h, k = divmod(i, KZ)
                    if i == 0:
                        for strip in range(GROUP):
                            pe.wait_ge(pairs_in[strip], 16 * GROUP * (n + 1))
                        pe.wait_ge(dense_ready, n + 1)
                    if i == K1 // 2 * KZ:
                        pe.wait_ge(y_ready, n + 1)
                    last = nc.tensor.matmul(ps_m[:, h, :], w1[:, k, P * h:P * h + P], pairs[:, :, k, :],
                                            start=(k == 0), stop=(k == KZ - 1))
                    if k == KZ - 1 and h % 2:
                        last.then_inc(layer1, 1)

            def layer_2(n, start, end):
                for i in range(start, end):
                    h, k = divmod(i, K1)
                    if i == 0:
                        pe.wait_ge(h1_ready, K1 * (n + 1))
                    last = nc.tensor.matmul(ps_2[:, h, :], w2_sb[:, k, P * h:P * h + P], h1[:, k, :],
                                            start=(k == 0), stop=(k == K1 - 1))
                if end == K1 * K2:
                    last.then_inc(layer2, 1)

            def layer_3(n):
                pe.wait_ge(h2_ready, K2 * (n + 1))
                for t in range(2):
                    for k in range(K2):
                        last = nc.tensor.matmul(ps_y[:, t:t + 1], h2[:, k, t, :], w3_sb[:, k:k + 1],
                                                start=(k == 0), stop=(k == K2 - 1))
                last.then_inc(layer3, 1)

            def block_step(n, mlp):
                select(n)
                plan = [0, 0, 2, 2, 2, 2] + [1] * BATCHES + [3, 3, 3, 3, 2, 2]
                ends = [sum(plan[:i + 1]) for i in range(len(plan))]
                for i, end in enumerate(ends):
                    if i < QUADS:
                        transpose_quad(n, 0, i, mlp)
                    elif i < QUADS + BATCHES:
                        gram_batch(n, 0, i - QUADS)
                    else:
                        transpose_quad(n, 1, i - QUADS - BATCHES, mlp)
                    if mlp:
                        layer_1(n - 1, end - plan[i], end)
                for m in range(BATCHES):
                    gram_batch(n, 1, m)
                    if mlp and 1 <= m <= 4:
                        layer_2(n - 1, 2 * m - 2, 2 * m)
                if mlp:
                    layer_3(n - 1)

            pe.wait_ge(ident_ready, 2)
            pe.wait_ge(zeros_ready, 1)
            pe.wait_ge(tables_ready, SEL)
            block_step(0, False)
            pe.wait_ge(w1_ready, 1)
            pe.wait_ge(weights_in, 6 * 16)
            with pe.Fori(1, BLOCKS) as n:
                block_step(n, True)
            layer_1(BLOCKS - 1, 0, K1 * KZ)
            layer_2(BLOCKS - 1, 0, K1 * K2)
            layer_3(BLOCKS - 1)

        @block.scalar
        def _(act):
            def shift_sel_idx(n):
                act.wait_ge(sel_idx_in, 16 * (n + 1))
                nc.scalar.activation(sel_idx[:, :, :], sel_idx[:, :, :].bitcast(I32), ACT.Identity,
                                     bias=first_row[:, 0:1]).then_inc(sel_idx_ready, 1)

            def round_selected(n, k):
                act.wait_ge(one_hot_used, ONE_HOTS * n + 2 * CHUNKS * (k + 1))
                nc.scalar.copy(sel_slots(0, k), sel_bank(k)).then_inc(sel_hi, 1)

            def round_tile(n, par):
                for q in range(QUADS):
                    act.wait_ge(transposed, QUADS * (2 * n + par) + q + 1)
                    nc.scalar.copy(quad_slots(0, par, q), quad_bank(q)[:, 0:len(quad(q)), :]).then_inc(et_hi, 1)

            def halve_gram(n, par, m):
                act.wait_ge(gram_ready, BATCHES * (2 * n + par) + m + 1)
                for i in range(GROUP):
                    nc.scalar.mul(gram_strip(par, m, i), diagonal(0, m, i), 0.5).then_inc(gram_half, 1)

            def relu_1(n, bank):
                act.wait_ge(layer1, K1 // 2 * n + bank + 1)
                for h in (2 * bank, 2 * bank + 1):
                    nc.scalar.activation(h1[:, h, :], ps_m[:, h, :], ACT.Relu, bias=b1_sb[:, h:h + 1]).then_inc(h1_ready, 1)

            def relu_2(n):
                act.wait_ge(layer2, n + 1)
                for h in range(K2):
                    nc.scalar.activation(h2[:, h, :, :].rearrange("p t (s i) -> p i t s", i=GROUP),
                                         ps_2[:, h, :].rearrange("p (i t s) -> p i t s", i=GROUP, t=2),
                                         ACT.Relu, bias=b2_sb[:, h:h + 1]).then_inc(h2_ready, 1)

            def block_step(n, mlp, more):
                for k in range(PAIRS):
                    round_selected(n, k)
                if mlp:
                    act.wait_ge(dense_ready, n)
                round_tile(n, 0)
                if mlp:
                    for i in range(GROUP):
                        act.wait_ge(pairs_in[i], 16 * GROUP * n)
                for m in range(BATCHES):
                    halve_gram(n, 0, m)
                if mlp:
                    relu_1(n - 1, 0)
                if more:
                    shift_sel_idx(n + 1)
                round_tile(n, 1)
                if mlp:
                    relu_1(n - 1, 1)
                for m in range(BATCHES):
                    halve_gram(n, 1, m)
                    if mlp and m == 5:
                        relu_2(n - 1)

            act.wait_ge(first_row_ready, 2)
            shift_sel_idx(0)
            for i in range(SEL):
                act.wait_ge(tables_in[i], 16)
                nc.scalar.copy(table_hi[:, i, :, :], raw_table(i)).then_inc(tables_hi_ready, 1)
            block_step(0, False, True)
            act.wait_ge(weights_in, 6 * 16)
            with act.Fori(1, BLOCKS - 1) as n:
                block_step(n, True, True)
            block_step(BLOCKS - 1, True, False)
            relu_1(BLOCKS - 1, 0)
            relu_1(BLOCKS - 1, 1)
            relu_2(BLOCKS - 1)

        @block.vector
        def _(dve):
            def rest_of_selected(n, k):
                dve.wait_ge(sel_hi, PAIRS * n + k + 1)
                nc.vector.tensor_tensor(sel_slots(1, k), sel_bank(k), sel_slots(0, k).bitcast(F32),
                                        ALU.subtract).then_inc(sel_lo, 1)

            def make_one_hots(n, start, end, first=False):
                if start == 0:
                    dve.wait_ge(sel_idx_ready, n + 1)
                for c in range(start, end):
                    if not first:
                        dve.wait_ge(one_hot_used, ONE_HOTS * n + c - RING + 1)
                    nc.vector.tensor_scalar(one_hot[:, c % RING, :], sel_idx[:, c // CHUNKS, :],
                                            float(c % CHUNKS), None, ALU.is_equal).then_inc(one_hot_ready, 1)
                    k = (c - RING // 2 + 1) // (2 * CHUNKS) - 1
                    if k >= 0 and (c - RING // 2 + 1) % (2 * CHUNKS) == 0:
                        rest_of_selected(n, k)
            def rest_of_quad(n, par, q):
                dve.wait_ge(et_hi, QUADS * (2 * n + par) + q + 1)
                nc.vector.tensor_tensor(quad_slots(1, par, q), quad_bank(q)[:, 0:len(quad(q)), :],
                                        quad_slots(0, par, q).bitcast(F32), ALU.subtract).then_inc(et_lo, 1)

            def empty_gram(n, par, m):
                for i in range(GROUP):
                    dve.wait_ge(gram_half, GROUP * (BATCHES * (2 * n + par) + m) + i + 1)
                    last = nc.vector.tensor_tensor(gram_strip(par, m, i), diagonal(1, m, i), gram_strip(par, m, i), ALU.add)
                last.then_inc(gram_out, 1)

            def add_dense(n):
                def slot_0(part):
                    return et[:, part, :, 0].rearrange("p (t s i) -> p i t s", t=2, i=GROUP).bitcast(F32)
                nc.vector.tensor_tensor(pairs[:, :, COLS, :].rearrange("p i (t s) -> p i t s", t=2),
                                        slot_0(0), slot_0(1), ALU.add).then_inc(dense_ready, 1)

            def keep_y(n):
                dve.wait_ge(layer3, n + 1)
                nc.vector.tensor_copy(y_sb[:, bass.ds(2 * n, 2)], ps_y).then_inc(y_ready, 1)

            def block_step(n, mlp, more):
                make_one_hots(n, RING, ONE_HOTS)
                rest_of_selected(n, PAIRS - 1)
                for q in range(QUADS):
                    rest_of_quad(n, 0, q)
                for m in range(BATCHES):
                    empty_gram(n, 0, m)
                for q in range(QUADS):
                    rest_of_quad(n, 1, q)
                    if more:
                        make_one_hots(n + 1, RING * q // QUADS, RING * (q + 1) // QUADS)
                for m in range(BATCHES):
                    empty_gram(n, 1, m)
                add_dense(n)
                if mlp:
                    keep_y(n - 1)

            nc.vector.memset(et[:, :, :, FEATS:WIDE].rearrange("p a b f -> p (a b) f").bitcast(F32), 0.0).then_inc(zeros_ready, 1)
            nc.vector.memset(y_sb[:, :], 0.0).then_inc(y_ready, 1)
            dve.wait_ge(first_row_ready, 1)
            nc.vector.tensor_copy(first_row[:, :], first_row_int[:, :]).then_inc(first_row_ready, 1)
            for i in range(SEL):
                dve.wait_ge(tables_hi_ready, i + 1)
                nc.vector.tensor_tensor(table_lo[:, i, :, :], raw_table(i), table_hi[:, i, :, :].bitcast(F32),
                                        ALU.subtract).then_inc(tables_ready, 1)
            make_one_hots(0, 0, RING, True)
            block_step(0, False, True)
            dve.wait_ge(weights_in, 6 * 16)
            nc.vector.tensor_tensor(w1[:, COLS, :], w1[:, COLS, :], w1[:, KZ, :], ALU.add).then_inc(w1_ready, 1)
            with dve.Fori(1, BLOCKS - 1) as n:
                block_step(n, True, True)
            block_step(BLOCKS - 1, True, False)
            keep_y(BLOCKS - 1)


def kernel(**inputs):
    import numpy as np
    import concourse.bacc as bacc
    from concourse.bass_utils import run_bass_kernel_spmd

    nc = bacc.Bacc("TRN2", target_bir_lowering=False, num_devices=1)
    w_top1 = np.asarray(inputs["W_top1"])
    a, b = np.triu_indices(FEATS, k=1)
    slot = np.array([0] + [1 + (GATHERED + SELECTED).index(t) for t in range(TABLES)])
    w_pairs = np.zeros((P, COLS, H1), w_top1.dtype)
    for f, g in ((slot[a], slot[b]), (slot[b], slot[a])):
        w_pairs[32 * (g // COLS) + f, g % COLS] = w_top1[P:P + len(a)]
    ids = np.asarray(inputs["ids"]).reshape(P, BLOCKS, 2, TABLES)
    arrays = {
        "x": inputs["r_dense_features"], "ids": inputs["ids"], "w_pairs": w_pairs,
        "sel_ids": ids[:, :, :, SELECTED].transpose(1, 3, 2, 0).reshape(BLOCKS, SEL, N),
        "w_dense": np.stack([w_top1[0:P], w_top1[P + len(a):]], axis=1),
        "b1": np.asarray(inputs["b_top1"]).reshape(K1, P).T, "w2": inputs["W_top2"],
        "b2": np.asarray(inputs["b_top2"]).reshape(K2, P).T,
        "w3": np.asarray(inputs["W_top3"]).reshape(K2, P).T,
    }
    arrays.update({f"tbl_{i}": inputs[f"tbl_{i}"] for i in range(TABLES)})
    arrays = {k: np.ascontiguousarray(v) for k, v in arrays.items()}
    ap = {k: nc.dram_tensor(k, v.shape, mybir.dt.from_np(v.dtype), kind="ExternalInput").ap() for k, v in arrays.items()}
    y = nc.dram_tensor("y", (TILES * P, 1), F32, kind="ExternalOutput").ap()
    dlrm(nc, ap["x"], ap["ids"], ap["sel_ids"], [ap[f"tbl_{i}"] for i in GATHERED],
         [ap[f"tbl_{i}"] for i in SELECTED], ap["w_dense"], ap["w_pairs"],
         ap["b1"], ap["w2"], ap["b2"], ap["w3"], y)
    return run_bass_kernel_spmd(nc, [arrays], core_ids=[0]).results[0]["y"]
```

```python
import concourse.bass as bass
from concourse import mybir
from contextlib import ExitStack

F32 = mybir.dt.float32
F32R = mybir.dt.float32r
I32 = mybir.dt.int32
ALU = mybir.AluOpType
ACT = mybir.ActivationFunctionType

P = 128
TABLES = 26
FEATS = TABLES + 1
SELECTED = [2, 6, 8, 9, 11, 13]
GATHERED = [t for t in range(TABLES) if t not in SELECTED]
TILES = 16
BLOCKS = TILES // 2
N = 2 * P

SLOTS = 28
WIDE = 32
ROWS = 1 + len(GATHERED)
QUAD = 4
QUADS = -(-ROWS // QUAD)

SEL = len(SELECTED)
SEL_ROWS = 1000
CHUNK = 125
CHUNKS = SEL_ROWS // CHUNK
PAIRS = SEL // 2
ONE_HOTS = SEL * CHUNKS
RING = 16

GROUP = 4
BATCH = 4
BATCHES = P // (GROUP * BATCH)
COLS = SLOTS // GROUP
HALF = P // GROUP
H1, H2 = 512, 256
K1, K2 = H1 // P, H2 // P
KZ = COLS + 1


def dlrm(nc, x, ids, sel_ids, gathered_tables, selected_tables, w_dense, w_pairs, b1, w2, b2, w3, y):
    x_v = x.rearrange("(p t) d -> p t d", t=TILES)
    ids_v = ids.rearrange("(p t) f -> p t f", t=TILES)

    ctx = ExitStack()
    with ctx:
        def sb(name, shape, dt=F32):
            return ctx.enter_context(nc.sbuf_tensor(name, shape, dt))

        def pb(name, shape):
            return ctx.enter_context(nc.psum_tensor(name, shape, F32))

        def sem(name):
            return ctx.enter_context(nc.semaphore(name))

        idx = [sb(f"idx{i}", [P, TABLES], I32) for i in range(2)]
        rows = [sb(f"rows{i}", [P, ROWS, P]) for i in range(2)]
        et = sb("et", [P, 2, N, WIDE], F32R)
        table_hi = sb("table_hi", [CHUNK, SEL, CHUNKS, P], F32R)
        table_lo = sb("table_lo", [CHUNK, SEL, CHUNKS, P], F32R)
        sel_idx = sb("sel_idx", [CHUNK, SEL, N])
        first_row = sb("first_row", [CHUNK, 1])
        first_row_int = sb("first_row_int", [CHUNK, 1], I32)
        one_hot = sb("one_hot", [CHUNK, RING, N], F32R)
        w1 = sb("w1", [P, KZ + 1, H1])
        w2_sb = sb("w2_sb", [P, K1, H2])
        w3_sb = sb("w3_sb", [P, K2])
        b1_sb = sb("b1_sb", [P, K1])
        b2_sb = sb("b2_sb", [P, K2])
        y_sb = sb("y_sb", [P, TILES])
        ident = sb("ident", [P, P])
        work = sb("work", [P, SEL * CHUNKS * P])
        ends = [0]
        for size in (SLOTS * 2 * HALF, GROUP * KZ * 2 * HALF, K1 * N, K2 * N):
            ends.append(ends[-1] + size)
        assert QUADS == 6 and PAIRS % 2 == 1 and ends[-1] <= SEL * CHUNKS * P
        gram = work[:, ends[0]:ends[1]].rearrange("p (g s) -> p g s", g=SLOTS)
        pairs = work[:, ends[1]:ends[2]].rearrange("p (i c s) -> p i c s", i=GROUP, c=KZ)
        h1 = work[:, ends[2]:ends[3]].rearrange("p (k n) -> p k n", k=K1)
        last_pairs = rows[0][:, :, :].rearrange("p f d -> p (f d)")[:, 0:2 * GROUP * KZ * HALF].rearrange(
            "p (t i c s) -> p t i c s", t=2, i=GROUP, c=KZ)
        h2 = work[:, ends[3]:ends[4]].rearrange("p (k t b) -> p k t b", k=K2, t=2)

        ps_t = [pb(f"ps_t{i}", [P, QUAD, P]) for i in range(2)]
        ps_g = [pb(f"ps_g{i}", [P, BATCH, N]) for i in range(2)]
        ps_m = pb("ps_m", [P, K1, N])
        ps_2 = ps_m[:, 0:K2, :]
        ps_y = ps_m[:, K2, 0:2]
        last_bank = [ps_t[0][:, 0, :], ps_t[1][:, 0, :], ps_g[0][:, 0, 0:P], ps_g[0][:, 2, 0:P],
                     ps_g[1][:, 0, 0:P], ps_g[1][:, 2, 0:P], ps_m[:, 0, 0:P], ps_m[:, 2, 0:P]]
        last_y = ps_g[1][:, 0, 0:2]

        weights_in = sem("weights_in")
        w1_ready = sem("w1_ready")
        ident_ready = sem("ident_ready")
        zeros_ready = sem("zeros_ready")
        first_row_ready = sem("first_row_ready")
        tables_in = [sem(f"tables_in{i}") for i in range(SEL)]
        tables_hi_ready = sem("tables_hi_ready")
        tables_ready = sem("tables_ready")
        idx_in = [sem(f"idx_in{i}") for i in range(2)]
        x_in = [sem(f"x_in{i}") for i in range(2)]
        gathered = [[sem(f"gathered{i}_{q}") for q in range(QUADS)] for i in range(2)]
        sel_idx_in = sem("sel_idx_in")
        sel_idx_ready = sem("sel_idx_ready")
        one_hot_ready = sem("one_hot_ready")
        one_hot_used = sem("one_hot_used")
        sel_hi = sem("sel_hi")
        sel_lo = sem("sel_lo")
        transposed = sem("transposed")
        et_hi = sem("et_hi")
        et_lo = sem("et_lo")
        gram_ready = sem("gram_ready")
        gram_half = sem("gram_half")
        gram_out = sem("gram_out")
        dense_ready = sem("dense_ready")
        pairs_in = [sem(f"pairs_in{i}") for i in range(GROUP)]
        MOVES = 16 * (GROUP - 1)
        kept = sem("kept")
        last_pairs_in = [sem(f"last_pairs_in{t}") for t in range(2)]
        last_strip_in = sem("last_strip_in")
        last_kept = sem("last_kept")
        last_dense = sem("last_dense")
        last_layer1 = sem("last_layer1")
        last_h1 = sem("last_h1")
        last_layer2 = sem("last_layer2")
        last_h2 = sem("last_h2")
        layer1 = sem("layer1")
        h1_ready = sem("h1_ready")
        layer2 = sem("layer2")
        h2_ready = sem("h2_ready")
        layer3 = sem("layer3")
        y_ready = sem("y_ready")
        y_out = sem("y_out")

        def quad_bank(q):
            if q in (0, QUADS - 1):
                return ps_t[q == 0][:, :, :]
            i, half = divmod(q - 1, 2)
            return ps_g[i][:, :, :].rearrange("p s c -> p (s c)")[:, 512 * half:512 * (half + 1)].rearrange(
                "p (q b) -> p q b", q=QUAD)

        def quad(q):
            return range(QUAD * q, min(QUAD * q + QUAD, ROWS))

        def quad_slots(part, par, q):
            return et[:, part, P * par:P * (par + 1), QUAD * q:QUAD * q + len(quad(q))].rearrange("p b f -> p f b")

        def sel_slots(part, k):
            return et[:, part, :, ROWS + 2 * k:ROWS + 2 * k + 2].rearrange("p b f -> p f b")

        def sel_bank(k):
            return ps_t[k % 2][:, :, :].rearrange("p q b -> p (q b)").rearrange("p (f b) -> p f b", f=2)

        def raw_table(i):
            return work[0:CHUNK, CHUNKS * P * i:CHUNKS * P * (i + 1)].rearrange("p (c d) -> p c d", c=CHUNKS)

        def gram_strip(par, m, i):
            s0 = HALF * par + BATCH * m
            return gram[32 * i:32 * i + 32, :, s0:s0 + BATCH].rearrange("p g s -> p s g")

        def diagonal(part, m, i):
            c = SLOTS * (GROUP * part + i)
            return ps_g[m % 2][32 * i:32 * i + 32, :, c:c + SLOTS]

        def strip_columns(i, j):
            return gram[32 * i:32 * i + 32, COLS * j:COLS * (j + 1), :]

        def move_strip(engine, n, i, arrived):
            engine.wait_ge(gram_out, 2 * BATCHES * (n + 1))
            for j in range(GROUP):
                if j != i:
                    engine.dma_start(pairs[32 * j:32 * j + 32, i, 0:COLS, :], strip_columns(i, j)).then_inc(arrived, 16)

        def move_last_strip(engine, t, i, arrived):
            engine.wait_ge(gram_out, BATCHES * (2 * BLOCKS - 1 + t))
            for j in range(GROUP):
                if j != i:
                    engine.dma_start(last_pairs[32 * j:32 * j + 32, t, i, 0:COLS, :],
                                     strip_columns(i, j)[:, :, HALF * t:HALF * (t + 1)]).then_inc(arrived, 16)

        block = ctx.enter_context(nc.Block())

        @block.sync
        def _(sp):
            def load_tile(par, tile):
                sp.dma_start(idx[par][:, :], ids_v[:, bass.ds(tile, 1), :].rearrange("p t f -> p (t f)")).then_inc(idx_in[par], 16)
                sp.dma_start(rows[par][:, 0, :], x_v[:, bass.ds(tile, 1), :].rearrange("p t d -> p (t d)")).then_inc(x_in[par], 16)

            def load_sel_idx(n):
                src = sel_ids[bass.ds(n, 1), :, :].rearrange("n f b -> n (f b)").broadcast_to([CHUNK, SEL * N])
                sp.dma_start(sel_idx[:, :, :].bitcast(I32), src.rearrange("p (f b) -> p f b", f=SEL)).then_inc(sel_idx_in, 16)

            load_sel_idx(0)
            load_tile(0, 0)
            for i in range(SEL):
                sp.dma_start(raw_table(i), selected_tables[i].rearrange("(p c) d -> p c d", p=CHUNK)).then_inc(tables_in[i], 16)
            load_tile(1, 1)
            sp.dma_start(w1[:, 0:COLS, :], w_pairs).then_inc(weights_in, 16)
            sp.dma_start(w1[:, COLS:KZ + 1, :], w_dense).then_inc(weights_in, 16)
            sp.dma_start(w2_sb[:, :, :], w2.rearrange("(k p) n -> p k n", p=P)).then_inc(weights_in, 16)
            sp.dma_start(b1_sb[:, :], b1).then_inc(weights_in, 16)
            sp.dma_start(b2_sb[:, :], b2).then_inc(weights_in, 16)
            sp.dma_start(w3_sb[:, :], w3).then_inc(weights_in, 16)
            with sp.Fori(0, BLOCKS - 1) as n:
                sp.wait_ge(one_hot_ready, ONE_HOTS * (n + 1))
                load_sel_idx(n + 1)
                for par in range(2):
                    sp.wait_ge(transposed, QUADS * (2 * n + par + 1))
                    load_tile(par, 2 * n + 2 + par)
                for i in range(GROUP):
                    move_strip(sp, n, i, pairs_in[i])
            for t in range(2):
                for i in range(GROUP - t):
                    move_last_strip(sp, t, i, last_pairs_in[t])
            sp.wait_ge(y_ready, BLOCKS + 1)
            sp.dma_start(y.rearrange("(p t) o -> p (t o)", t=TILES), y_sb[:, :]).then_inc(y_out, 16)
            sp.wait_ge(y_out, 16)

        @block.gpsimd
        def _(pool):
            pool.memset(ident[:, :], 0.0).then_inc(ident_ready, 1)
            pool.wait_ge(ident_ready, 1)
            pool.affine_select(out=ident[:, :], in_=ident[:, :], compare_op=ALU.not_equal, fill=1.0,
                               base=0, pattern=[[-1, P]], channel_multiplier=1).then_inc(ident_ready, 1)
            pool.iota(first_row_int[:, :], pattern=[[1, 1]], base=0, channel_multiplier=-CHUNKS).then_inc(first_row_ready, 1)

            def gather_tile(par, uses, freed):
                pool.wait_ge(idx_in[par], 16 * uses)
                pool.nop(nofuse=True)
                for q in range(QUADS):
                    if freed is not None:
                        pool.wait_ge(transposed, freed + q + 1)
                        pool.nop(nofuse=True)
                    for f in quad(q):
                        if f:
                            table = GATHERED[f - 1]
                            pool.indirect_dma_start(
                                rows[par][:, f, :], None, gathered_tables[f - 1],
                                bass.IndirectOffsetOnAxis(idx[par][:, table:table + 1], 0)).then_inc(gathered[par][q], 16)

            for par in range(2):
                gather_tile(par, 1, None)
            with pool.Fori(0, BLOCKS - 1) as m:
                for par in range(2):
                    gather_tile(par, m + 2, QUADS * (2 * m + par))
            move_last_strip(pool, 1, GROUP - 1, last_strip_in)

        @block.tensor
        def _(pe):
            def select(n, start, end, first=False):
                for c in range(start, end):
                    k, f = c // (2 * CHUNKS), c // CHUNKS
                    if first and c % CHUNKS == 0:
                        pe.wait_ge(tables_ready, f + 1)
                    if k >= 2 and c % (2 * CHUNKS) == 0:
                        pe.wait_ge(sel_lo, PAIRS * n + k - 1)
                    pe.wait_ge(one_hot_ready, ONE_HOTS * n + c + 1)
                    out = sel_bank(k)[:, f % 2, :]
                    nc.tensor.matmul(out, table_hi[:, f, c % CHUNKS, :], one_hot[:, c % RING, :],
                                     start=(c % CHUNKS == 0), stop=False)
                    nc.tensor.matmul(out, table_lo[:, f, c % CHUNKS, :], one_hot[:, c % RING, :],
                                     start=False, stop=(c % CHUNKS == CHUNKS - 1)).then_inc(one_hot_used, 1)

            def transpose_quad(n, par, q, later):
                if q == 0:
                    pe.wait_ge(x_in[par], 16 * (n + 1))
                pe.wait_ge(gathered[par][q], 16 * (len(quad(q)) - (q == 0)) * (n + 1))
                if par == 0 and q in (0, QUADS - 1):
                    pe.wait_ge(sel_lo, PAIRS * n + (PAIRS - 1 if q == 0 else PAIRS))
                if (par or later) and q in (1, 3):
                    pe.wait_ge(gram_out, BATCHES * (2 * n + par) - 1 + q // 2)
                for f in quad(q):
                    last = nc.tensor.transpose(quad_bank(q)[:, f % QUAD, :], rows[par][:, f, :], ident[:, :])
                last.then_inc(transposed, 1)

            def gram_batch(n, par, m):
                if m == 0:
                    pe.wait_ge(et_lo, QUADS * (2 * n + par + 1))
                if m >= 2:
                    pe.wait_ge(gram_out, BATCHES * (2 * n + par) + m - 1)
                for s in range(BATCH):
                    b = P * par + GROUP * (BATCH * m + s)
                    last = nc.tensor.matmul(
                        ps_g[m % 2][:, s, 0:2 * GROUP * SLOTS].rearrange("p (a b f) -> p a b f", a=2, b=GROUP),
                        et[:, 0, b:b + GROUP, :].rearrange("p b f -> p (b f)"),
                        et[:, :, b:b + GROUP, 0:SLOTS], start=True, stop=True)
                last.then_inc(gram_ready, 1)

            def layer_1(n, start, end):
                for i in range(start, end):
                    h, k = divmod(i, KZ)
                    if i == 0:
                        for strip in range(GROUP):
                            pe.wait_ge(pairs_in[strip], MOVES * (n + 1))
                        pe.wait_ge(kept, GROUP * (n + 1))
                        pe.wait_ge(dense_ready, n + 1)
                    if i == K1 // 2 * KZ:
                        pe.wait_ge(y_ready, n + 1)
                    product = nc.tensor.matmul(ps_m[:, h, :], w1[:, k, P * h:P * h + P], pairs[:, :, k, :],
                                            start=(k == 0), stop=(k == KZ - 1))
                    if k == KZ - 1 and h % 2:
                        product.then_inc(layer1, 1)

            def layer_2(n, start, end):
                for i in range(start, end):
                    h, k = divmod(i, K1)
                    if i == 0:
                        pe.wait_ge(h1_ready, K1 * (n + 1))
                    last = nc.tensor.matmul(ps_2[:, h, :], w2_sb[:, k, P * h:P * h + P], h1[:, k, :],
                                            start=(k == 0), stop=(k == K1 - 1))
                if end == K1 * K2:
                    last.then_inc(layer2, 1)

            def layer_3(n):
                pe.wait_ge(h2_ready, K2 * (n + 1))
                for t in range(2):
                    for k in range(K2):
                        last = nc.tensor.matmul(ps_y[:, t:t + 1], h2[:, k, t, :], w3_sb[:, k:k + 1],
                                                start=(k == 0), stop=(k == K2 - 1))
                last.then_inc(layer3, 1)

            def last_layer_1(t, h):
                if h == 0:
                    pe.wait_ge(last_pairs_in[t], MOVES * (GROUP - t))
                    if t == 1:
                        pe.wait_ge(last_strip_in, MOVES)
                        pe.wait_ge(y_ready, BLOCKS)
                    pe.wait_ge(last_kept, GROUP * (t + 1))
                    pe.wait_ge(last_dense, t + 1)
                if t == 0 and h == 2:
                    pe.wait_ge(gram_out, 2 * BATCHES * BLOCKS)
                for k in range(KZ):
                    product = nc.tensor.matmul(last_bank[K1 * t + h], w1[:, k, P * h:P * h + P], last_pairs[:, t, :, k, :],
                                               start=(k == 0), stop=(k == KZ - 1))
                product.then_inc(last_layer1, 1)

            def last_layer_2(t):
                for h in range(K2):
                    for k in range(K1):
                        if h == 0:
                            pe.wait_ge(last_h1, max(K2 * (t + 1), K1 * t + k + 1))
                        product = nc.tensor.matmul(last_bank[K2 * t + h], w2_sb[:, k, P * h:P * h + P],
                                                   h1[:, k, P * t:P * (t + 1)], start=(k == 0), stop=(k == K1 - 1))
                    product.then_inc(last_layer2, 1)

            def last_layer_3(t):
                for k in range(K2):
                    pe.wait_ge(last_h2, K2 * t + k + 1)
                    product = nc.tensor.matmul(last_y[:, t:t + 1], h2[:, k, t, :], w3_sb[:, k:k + 1],
                                               start=(k == 0), stop=(k == K2 - 1))
                if t == 1:
                    product.then_inc(layer3, 1)

            def block_step(n, mlp, more):
                select(n, 2 * CHUNKS, ONE_HOTS, not mlp)
                plan = [0, 0, 0, 2, 4, 4] + [1] * BATCHES + ([3, 3, 3, 1, 1, 3] if more else [0, 0, 1, 1, 2, 2])
                ends = [sum(plan[:i + 1]) for i in range(len(plan))]
                for i, end in enumerate(ends):
                    if i < QUADS:
                        transpose_quad(n, 0, i, mlp)
                    elif i < QUADS + BATCHES:
                        gram_batch(n, 0, i - QUADS)
                    else:
                        transpose_quad(n, 1, i - QUADS - BATCHES, mlp)
                    if mlp:
                        layer_1(n - 1, end - plan[i], end)
                ahead = (0, 4, 8, 2 * CHUNKS)
                done = ends[-1]
                for m in range(BATCHES):
                    gram_batch(n, 1, m)
                    if not more:
                        layer_1(n - 1, done + m, done + m + 1)
                    elif mlp and 1 <= m <= 4:
                        layer_2(n - 1, 2 * m - 2, 2 * m)
                    if more and m >= 5:
                        first, end = ahead[m - 5:m - 3]
                        select(n + 1, first, end)
                if not more:
                    last_layer_1(0, 0)
                    layer_2(n - 1, 0, K1 * K2)
                    last_layer_1(0, 1)
                if mlp:
                    layer_3(n - 1)

            pe.wait_ge(ident_ready, 2)
            pe.wait_ge(zeros_ready, 1)
            select(0, 0, 2 * CHUNKS, True)
            block_step(0, False, True)
            pe.wait_ge(w1_ready, 1)
            pe.wait_ge(weights_in, 6 * 16)
            with pe.Fori(1, BLOCKS - 1) as n:
                block_step(n, True, True)
            block_step(BLOCKS - 1, True, False)
            for t in range(2):
                for h in range(2 * (1 - t), K1):
                    last_layer_1(t, h)
            for t in range(2):
                last_layer_2(t)
            for t in range(2):
                last_layer_3(t)

        @block.scalar
        def _(act):
            def shift_sel_idx(n, f):
                act.wait_ge(sel_idx_in, 16 * (n + 1))
                nc.scalar.activation(sel_idx[:, f, :], sel_idx[:, f, :].bitcast(I32), ACT.Identity,
                                     bias=first_row[:, 0:1]).then_inc(sel_idx_ready, 1)

            def round_selected(n, k):
                act.wait_ge(one_hot_used, ONE_HOTS * n + 2 * CHUNKS * (k + 1))
                nc.scalar.copy(sel_slots(0, k), sel_bank(k)).then_inc(sel_hi, 1)

            def round_tile(n, par, more=False):
                for q in range(QUADS):
                    act.wait_ge(transposed, QUADS * (2 * n + par) + q + 1)
                    nc.scalar.copy(quad_slots(0, par, q), quad_bank(q)[:, 0:len(quad(q)), :]).then_inc(et_hi, 1)
                    if more and q < SEL - 2:
                        shift_sel_idx(n + 1, 2 + q)

            def halve_gram(n, par, m):
                act.wait_ge(gram_ready, BATCHES * (2 * n + par) + m + 1)
                for i in range(GROUP):
                    nc.scalar.mul(gram_strip(par, m, i), diagonal(0, m, i), 0.5).then_inc(gram_half, 1)

            def keep_strips(n):
                act.wait_ge(gram_out, 2 * BATCHES * (n + 1))
                for i in range(GROUP):
                    nc.scalar.copy(pairs[32 * i:32 * i + 32, i, 0:COLS, :], strip_columns(i, i)).then_inc(kept, 1)

            def keep_last_strips(t):
                act.wait_ge(gram_out, BATCHES * (2 * BLOCKS - 1 + t))
                for i in range(GROUP):
                    nc.scalar.copy(last_pairs[32 * i:32 * i + 32, t, i, 0:COLS, :],
                                   strip_columns(i, i)[:, :, HALF * t:HALF * (t + 1)]).then_inc(last_kept, 1)

            def relu_1(n, bank):
                act.wait_ge(layer1, K1 // 2 * n + bank + 1)
                for h in (2 * bank, 2 * bank + 1):
                    nc.scalar.activation(h1[:, h, :], ps_m[:, h, :], ACT.Relu, bias=b1_sb[:, h:h + 1]).then_inc(h1_ready, 1)

            def relu_2(n):
                act.wait_ge(layer2, n + 1)
                for h in range(K2):
                    nc.scalar.activation(h2[:, h, :, :].rearrange("p t (s i) -> p i t s", i=GROUP),
                                         ps_2[:, h, :].rearrange("p (i t s) -> p i t s", i=GROUP, t=2),
                                         ACT.Relu, bias=b2_sb[:, h:h + 1]).then_inc(h2_ready, 1)

            def block_step(n, mlp, more):
                round_selected(n, 0)
                if mlp:
                    keep_strips(n - 1)
                round_selected(n, 1)
                round_selected(n, 2)
                if mlp:
                    act.wait_ge(dense_ready, n)
                round_tile(n, 0)
                if mlp:
                    for i in range(GROUP):
                        act.wait_ge(pairs_in[i], MOVES * n)
                for m in range(BATCHES):
                    halve_gram(n, 0, m)
                    if more and m in (4, 7):
                        shift_sel_idx(n + 1, (m - 4) // 3)
                    if mlp and m == 6:
                        relu_1(n - 1, 0)
                round_tile(n, 1, more)
                if not more:
                    keep_last_strips(0)
                elif mlp:
                    relu_1(n - 1, 1)
                for m in range(BATCHES):
                    halve_gram(n, 1, m)
                    if mlp and more and m == 6:
                        relu_2(n - 1)

            act.wait_ge(first_row_ready, 2)
            for i in range(SEL):
                shift_sel_idx(0, i)
                act.wait_ge(tables_in[i], 16)
                nc.scalar.copy(table_hi[:, i, :, :], raw_table(i)).then_inc(tables_hi_ready, 1)
            block_step(0, False, True)
            act.wait_ge(weights_in, 6 * 16)
            with act.Fori(1, BLOCKS - 1) as n:
                block_step(n, True, True)
            block_step(BLOCKS - 1, True, False)
            relu_1(BLOCKS - 2, 1)
            keep_last_strips(1)
            relu_2(BLOCKS - 2)
            for t in range(2):
                for h in range(K1):
                    act.wait_ge(last_layer1, K1 * t + h + 1)
                    nc.scalar.activation(h1[:, h, P * t:P * (t + 1)], last_bank[K1 * t + h],
                                         ACT.Relu, bias=b1_sb[:, h:h + 1]).then_inc(last_h1, 1)
            for t in range(2):
                for h in range(K2):
                    act.wait_ge(last_layer2, K2 * t + h + 1)
                    nc.scalar.activation(h2[:, h, t, :].rearrange("p (s i) -> p i s", i=GROUP),
                                         last_bank[K2 * t + h].rearrange("p (i s) -> p i s", i=GROUP),
                                         ACT.Relu, bias=b2_sb[:, h:h + 1]).then_inc(last_h2, 1)

        @block.vector
        def _(dve):
            def rest_of_selected(n, k):
                dve.wait_ge(sel_hi, PAIRS * n + k + 1)
                nc.vector.tensor_tensor(sel_slots(1, k), sel_bank(k), sel_slots(0, k).bitcast(F32),
                                        ALU.subtract).then_inc(sel_lo, 1)

            LATER = 12

            def make_one_hots(n, start, end, first=False):
                for c in range(start, end):
                    if c % CHUNKS == 0:
                        dve.wait_ge(sel_idx_ready, SEL * n + c // CHUNKS + 1)
                    if not first:
                        dve.wait_ge(one_hot_used, ONE_HOTS * n + c - RING + 1)
                    nc.vector.tensor_scalar(one_hot[:, c % RING, :], sel_idx[:, c // CHUNKS, :],
                                            float(c % CHUNKS), None, ALU.is_equal).then_inc(one_hot_ready, 1)
                    k = (c - LATER + 1) // (2 * CHUNKS) - 1
                    if k >= 0 and (c - LATER + 1) % (2 * CHUNKS) == 0:
                        rest_of_selected(n, k)
            def rest_of_quad(n, par, q):
                dve.wait_ge(et_hi, QUADS * (2 * n + par) + q + 1)
                nc.vector.tensor_tensor(quad_slots(1, par, q), quad_bank(q)[:, 0:len(quad(q)), :],
                                        quad_slots(0, par, q).bitcast(F32), ALU.subtract).then_inc(et_lo, 1)

            def empty_gram(n, par, m):
                for i in range(GROUP):
                    dve.wait_ge(gram_half, GROUP * (BATCHES * (2 * n + par) + m) + i + 1)
                    last = nc.vector.tensor_tensor(gram_strip(par, m, i), diagonal(1, m, i), gram_strip(par, m, i), ALU.add)
                last.then_inc(gram_out, 1)

            def add_dense(n):
                def slot_0(part):
                    return et[:, part, :, 0].rearrange("p (t s i) -> p i t s", t=2, i=GROUP).bitcast(F32)
                nc.vector.tensor_tensor(pairs[:, :, COLS, :].rearrange("p i (t s) -> p i t s", t=2),
                                        slot_0(0), slot_0(1), ALU.add).then_inc(dense_ready, 1)

            def add_last_dense(t):
                def slot_0(part):
                    return et[:, part, P * t:P * (t + 1), 0].rearrange("p (s i) -> p i s", i=GROUP).bitcast(F32)
                nc.vector.tensor_tensor(last_pairs[:, t, :, COLS, :], slot_0(0), slot_0(1), ALU.add).then_inc(last_dense, 1)

            def keep_y(n, bank):
                dve.wait_ge(layer3, n + 1)
                nc.vector.tensor_copy(y_sb[:, bass.ds(2 * n, 2)], bank).then_inc(y_ready, 1)

            def block_step(n, mlp, more):
                make_one_hots(n, 2 * RING, ONE_HOTS)
                rest_of_selected(n, PAIRS - 1)
                for q in range(QUADS):
                    rest_of_quad(n, 0, q)
                for m in range(BATCHES):
                    empty_gram(n, 0, m)
                for q in range(QUADS):
                    rest_of_quad(n, 1, q)
                    if more and q < 3:
                        make_one_hots(n + 1, RING * q // 3, RING * (q + 1) // 3)
                if not more:
                    add_last_dense(0)
                for m in range(BATCHES):
                    empty_gram(n, 1, m)
                if more:
                    make_one_hots(n + 1, RING, 2 * RING)
                if more:
                    add_dense(n)
                else:
                    add_last_dense(1)
                if mlp:
                    keep_y(n - 1, ps_y)

            nc.vector.memset(et[:, :, :, FEATS:WIDE].rearrange("p a b f -> p (a b) f").bitcast(F32), 0.0).then_inc(zeros_ready, 1)
            nc.vector.memset(y_sb[:, :], 0.0).then_inc(y_ready, 1)
            dve.wait_ge(first_row_ready, 1)
            nc.vector.tensor_copy(first_row[:, :], first_row_int[:, :]).then_inc(first_row_ready, 1)
            for i in range(SEL):
                dve.wait_ge(tables_hi_ready, i + 1)
                nc.vector.tensor_tensor(table_lo[:, i, :, :], raw_table(i), table_hi[:, i, :, :].bitcast(F32),
                                        ALU.subtract).then_inc(tables_ready, 1)
                if i < 2:
                    make_one_hots(0, CHUNKS * i, CHUNKS * (i + 1), True)
            make_one_hots(0, RING, 2 * RING)
            block_step(0, False, True)
            dve.wait_ge(weights_in, 6 * 16)
            nc.vector.tensor_tensor(w1[:, COLS, :], w1[:, COLS, :], w1[:, KZ, :], ALU.add).then_inc(w1_ready, 1)
            with dve.Fori(1, BLOCKS - 1) as n:
                block_step(n, True, True)
            block_step(BLOCKS - 1, True, False)
            keep_y(BLOCKS - 1, last_y)


def kernel(**inputs):
    import numpy as np
    import concourse.bacc as bacc
    from concourse.bass_utils import run_bass_kernel_spmd

    nc = bacc.Bacc("TRN2", target_bir_lowering=False, num_devices=1)
    w_top1 = np.asarray(inputs["W_top1"])
    a, b = np.triu_indices(FEATS, k=1)
    slot = np.array([0] + [1 + (GATHERED + SELECTED).index(t) for t in range(TABLES)])
    w_pairs = np.zeros((P, COLS, H1), w_top1.dtype)
    for f, g in ((slot[a], slot[b]), (slot[b], slot[a])):
        w_pairs[32 * (g // COLS) + f, g % COLS] = w_top1[P:P + len(a)]
    ids = np.asarray(inputs["ids"]).reshape(P, BLOCKS, 2, TABLES)
    arrays = {
        "x": inputs["r_dense_features"], "ids": inputs["ids"], "w_pairs": w_pairs,
        "sel_ids": ids[:, :, :, SELECTED].transpose(1, 3, 2, 0).reshape(BLOCKS, SEL, N),
        "w_dense": np.stack([w_top1[0:P], w_top1[P + len(a):]], axis=1),
        "b1": np.asarray(inputs["b_top1"]).reshape(K1, P).T, "w2": inputs["W_top2"],
        "b2": np.asarray(inputs["b_top2"]).reshape(K2, P).T,
        "w3": np.asarray(inputs["W_top3"]).reshape(K2, P).T,
    }
    arrays.update({f"tbl_{i}": inputs[f"tbl_{i}"] for i in range(TABLES)})
    arrays = {k: np.ascontiguousarray(v) for k, v in arrays.items()}
    ap = {k: nc.dram_tensor(k, v.shape, mybir.dt.from_np(v.dtype), kind="ExternalInput").ap() for k, v in arrays.items()}
    y = nc.dram_tensor("y", (TILES * P, 1), F32, kind="ExternalOutput").ap()
    dlrm(nc, ap["x"], ap["ids"], ap["sel_ids"], [ap[f"tbl_{i}"] for i in GATHERED],
         [ap[f"tbl_{i}"] for i in SELECTED], ap["w_dense"], ap["w_pairs"],
         ap["b1"], ap["w2"], ap["b2"], ap["w3"], y)
    return run_bass_kernel_spmd(nc, [arrays], core_ids=[0]).results[0]["y"]
```
